# Optimizing a Trainium2 kernel written in Bass

```python
import numpy as np
import jax
import jax.numpy as jnp

def _softmax(x, axis=-1):
    return jax.nn.softmax(x, axis=axis)

def _gelu(x):
    return jax.nn.gelu(x, approximate=True)

def _silu(x):
    return jax.nn.silu(x)

def _sigmoid(x):
    return jax.nn.sigmoid(x)

def _layernorm(x, axis=-1, eps=1e-05):
    m = jnp.mean(x, axis=axis, keepdims=True)
    v = jnp.var(x, axis=axis, keepdims=True)
    return (x - m) / jnp.sqrt(v + eps)

def _scatter_add(tgt, idx, src, axis=0):
    return tgt.at[idx].add(src)

def _segment_sum(src, seg, n):
    return jax.ops.segment_sum(src, seg, n)
kernel_name = 'mk_gps_d1_gnn_r8_d4aab4'

def setup_inputs(seed: int=0):
    np.random.seed(seed)
    _w = jnp.asarray

    def _rec_inputs():
        import jax
        import jax.numpy as jnp
        _gk = jax.random.key(seed)
        x = -0.0003019 + 1 * jax.random.normal(jax.random.fold_in(_gk, 1), (2500, 1024), jnp.float32)
        src = jax.random.randint(jax.random.fold_in(_gk, 2), (80000,), 0, 2500, jnp.int32)
        dst = jax.random.randint(jax.random.fold_in(_gk, 3), (80000,), 0, 2500, jnp.int32)
        _o = jnp.argsort(dst, stable=True)
        src = src[_o]
        dst = dst[_o]
        return (x, src, dst)
    x, src, dst = _rec_inputs()

    def _L0_gnn_setup():
        import jax, jax.numpy as jnp
        import numpy as np
        N, IN_FEAT, OUT_FEAT, HEADS, E = (2500, 1024, 256, 4, 40000)
        NEG_SLOPE = 0.2
        key = jax.random.key(seed)
        k1, k2, k3, k4, k5, k6 = jax.random.split(key, 6)
        h = jax.random.normal(k1, (N, IN_FEAT), dtype=jnp.float32)
        src = jax.random.randint(k2, (E,), 0, N, dtype=jnp.int32)
        dst = jax.random.randint(k3, (E,), 0, N, dtype=jnp.int32)
        W = jax.random.normal(k4, (HEADS, IN_FEAT, OUT_FEAT), dtype=jnp.float32) * (1.0 / np.sqrt(IN_FEAT))
        a_l = jax.random.normal(k5, (HEADS, OUT_FEAT), dtype=jnp.float32) * (1.0 / np.sqrt(OUT_FEAT))
        a_r = jax.random.normal(k6, (HEADS, OUT_FEAT), dtype=jnp.float32) * (1.0 / np.sqrt(OUT_FEAT))
        return {'h': h, 'W': W, 'a_l': a_l, 'a_r': a_r, 'src': src, 'dst': dst}
    _L0_gnn_all = _L0_gnn_setup()
    _L0_gnn_in = {k: v for k, v in _L0_gnn_all.items() if k in ('W', 'a_l', 'a_r')}
    del _L0_gnn_all

    def _L0_mix_setup():
        import jax, jax.numpy as jnp
        import numpy as np
        DIM = 1024
        HEADS = 16
        HEAD_DIM = DIM // HEADS
        key = jax.random.key(seed)
        k1, k2, k3, k4 = jax.random.split(key, 4)
        x = jax.random.normal(k1, (4, 512, DIM), dtype=jnp.float32)
        w_qkv = jax.random.normal(k2, (3 * DIM, DIM), dtype=jnp.float32) * DIM ** (-0.5)
        w_proj = jax.random.normal(k3, (DIM, DIM), dtype=jnp.float32) * DIM ** (-0.5)
        b_proj = jax.random.normal(k4, (DIM,), dtype=jnp.float32) * 0.01
        return {'x': x, 'w_qkv': w_qkv, 'w_proj': w_proj, 'b_proj': b_proj}
    _L0_mix_all = _L0_mix_setup()
    _L0_mix_in = {k: v for k, v in _L0_mix_all.items() if k in ('w_qkv', 'w_proj', 'b_proj')}
    del _L0_mix_all

    def _L0_ffn_setup():
        import jax, jax.numpy as jnp
        import numpy as np
        QMAX = 127.0

        def _ste_round(v):
            return v + jax.lax.stop_gradient(jnp.round(v) - v)

        def _act_fake_quant(x, clip_factor):
            scale = jax.nn.sigmoid(clip_factor) * jnp.max(jnp.abs(x)) / QMAX
            return jnp.clip(_ste_round(x / scale), -QMAX - 1.0, QMAX) * scale

        def _weight_fake_quant(w):
            scale = jnp.max(jnp.abs(w), axis=1, keepdims=True) / QMAX
            return jnp.clip(_ste_round(w / scale), -QMAX - 1.0, QMAX) * scale
        key = jax.random.key(seed)
        k1, k2, k3, k4 = jax.random.split(key, 4)
        B, S, H, I = (8, 1024, 1024, 352)
        return {'x': jax.random.normal(k1, (B, S, H), dtype=jnp.float32), 'clip_x': jnp.full((1,), 4.0, dtype=jnp.float32), 'clip_down': jnp.full((1,), 4.0, dtype=jnp.float32), 'w_gate': jax.random.normal(k2, (I, H), dtype=jnp.float32) * 0.02, 'w_up': jax.random.normal(k3, (I, H), dtype=jnp.float32) * 0.02, 'w_down': jax.random.normal(k4, (H, I), dtype=jnp.float32) * 0.02}
    _L0_ffn_all = _L0_ffn_setup()
    _L0_ffn_in = {k: v for k, v in _L0_ffn_all.items() if k in ('clip_x', 'clip_down', 'w_gate', 'w_up', 'w_down')}
    del _L0_ffn_all
    return {'x': x, 'src': src, 'dst': dst, 'L0_gnn_W': _L0_gnn_in['W'], 'L0_gnn_a_l': _L0_gnn_in['a_l'], 'L0_gnn_a_r': _L0_gnn_in['a_r'], 'L0_mix_w_qkv': _L0_mix_in['w_qkv'], 'L0_mix_w_proj': _L0_mix_in['w_proj'], 'L0_mix_b_proj': _L0_mix_in['b_proj'], 'L0_ffn_clip_x': _L0_ffn_in['clip_x'], 'L0_ffn_clip_down': _L0_ffn_in['clip_down'], 'L0_ffn_w_gate': _L0_ffn_in['w_gate'], 'L0_ffn_w_up': _L0_ffn_in['w_up'], 'L0_ffn_w_down': _L0_ffn_in['w_down']}

def reference(x, src, dst, L0_gnn_W, L0_gnn_a_l, L0_gnn_a_r, L0_mix_w_qkv, L0_mix_w_proj, L0_mix_b_proj, L0_ffn_clip_x, L0_ffn_clip_down, L0_ffn_w_gate, L0_ffn_w_up, L0_ffn_w_down):
    import jax
    import jax.numpy as jnp

    def _L0_gnn_ref(h, W, a_l, a_r, src, dst):
        import jax, jax.numpy as jnp
        import numpy as np
        N, IN_FEAT, OUT_FEAT, HEADS, E = (2500, 1024, 256, 4, 40000)
        NEG_SLOPE = 0.2
        z = jnp.einsum('ni,hif->nhf', h, W)
        el = jnp.einsum('nhf,hf->nh', z, a_l)
        er = jnp.einsum('nhf,hf->nh', z, a_r)
        e = jax.nn.leaky_relu(el[src] + er[dst], NEG_SLOPE)
        m = jax.ops.segment_max(e, dst, num_segments=N)
        ex = jnp.exp(e - m[dst])
        s = jax.ops.segment_sum(ex, dst, num_segments=N)
        alpha = ex / s[dst]
        out = jax.ops.segment_sum(alpha[:, :, None] * z[src], dst, num_segments=N)
        return out.reshape(N, HEADS * OUT_FEAT)

    def _L0_mix_ref(x, w_qkv, w_proj, b_proj):
        import jax, jax.numpy as jnp
        import numpy as np
        DIM = 1024
        HEADS = 16
        HEAD_DIM = DIM // HEADS
        B, N, C = x.shape
        H, D = (HEADS, HEAD_DIM)
        qkv = x @ w_qkv.T
        qkv = qkv.reshape(B, N, 3, H, D).transpose(2, 0, 3, 1, 4)
        q, k, v = (qkv[0], qkv[1], qkv[2])
        q = jax.nn.elu(q) + 1.0
        k = jax.nn.elu(k) + 1.0
        kv = jnp.einsum('bhnd,bhne->bhde', k, v)
        num = jnp.einsum('bhnd,bhde->bhne', q, kv)
        k_sum = k.sum(axis=-2)
        qk = jnp.einsum('bhnd,bhd->bhn', q, k_sum)[..., None]
        out = num / (qk + 1e-08)
        out = out.transpose(0, 2, 1, 3).reshape(B, N, C)
        return out @ w_proj.T + b_proj

    def _L0_ffn_ref(x, clip_x, clip_down, w_gate, w_up, w_down):
        import jax, jax.numpy as jnp
        import numpy as np
        QMAX = 127.0

        def _ste_round(v):
            return v + jax.lax.stop_gradient(jnp.round(v) - v)

        def _act_fake_quant(x, clip_factor):
            scale = jax.nn.sigmoid(clip_factor) * jnp.max(jnp.abs(x)) / QMAX
            return jnp.clip(_ste_round(x / scale), -QMAX - 1.0, QMAX) * scale

        def _weight_fake_quant(w):
            scale = jnp.max(jnp.abs(w), axis=1, keepdims=True) / QMAX
            return jnp.clip(_ste_round(w / scale), -QMAX - 1.0, QMAX) * scale
        xq = _act_fake_quant(x, clip_x[0])
        gate = jnp.einsum('bsh,ih->bsi', xq, _weight_fake_quant(w_gate))
        up = jnp.einsum('bsh,ih->bsi', xq, _weight_fake_quant(w_up))
        h = _act_fake_quant(jax.nn.silu(gate) * up, clip_down[0])
        return jnp.einsum('bsi,hi->bsh', h, _weight_fake_quant(w_down))
    xn = _layernorm(x, axis=-1)
    x = x + _L0_gnn_ref(xn, L0_gnn_W, L0_gnn_a_l, L0_gnn_a_r, src, dst) + _L0_mix_ref(xn[None], L0_mix_w_qkv, L0_mix_w_proj, L0_mix_b_proj)[0]
    x = x + _L0_ffn_ref(_layernorm(x, axis=-1)[None], L0_ffn_clip_x, L0_ffn_clip_down, L0_ffn_w_gate, L0_ffn_w_up, L0_ffn_w_down)[0]
    return x

_drawn_inputs = setup_inputs


def setup_inputs(seed=0):
    import zlib

    import numpy as np

    out = dict(_drawn_inputs(seed))
    spreads = {}
    factors = {'L0_mix_b_proj': 4.624}
    for name, (base, spread) in spreads.items():
        noise = np.random.default_rng([zlib.crc32(name.encode()), seed]).standard_normal(out[name].shape)
        drawn = base * np.exp(spread * noise) if base else spread * noise
        out[name] = jnp.asarray(drawn.astype(out[name].dtype))
    for name, factor in factors.items():
        out[name] = (out[name] * factor).astype(out[name].dtype)
    return out
```

```python
from contextlib import ExitStack

import concourse.bass as bass
from concourse import mybir

F32 = mybir.dt.float32
F32R = mybir.dt.float32r
BF16 = mybir.dt.bfloat16
I32 = mybir.dt.int32
U32 = mybir.dt.uint32
BYTES = {F32: 4, F32R: 4, BF16: 2, I32: 4, U32: 4}
ALU = mybir.AluOpType
ACT = mybir.ActivationFunctionType
AX = mybir.AxisListType

N = 2500
D = 1024
E = 80000
P = 128
TP = 125
NT = N // TP
KT = D // P
HALF = 512
GH = 4
GF = 256
ZW = GF + 1
AH = 16
AD = 64
CW = 500
NC = N // CW
JT = CW // TP
FI = 352
IB = [(0, 128), (128, 128), (256, 96)]
FIP = 384
GU = 2 * FIP // P
EPS = 1e-5
SLOPE = 0.2
QMAX = 127.0
MAGIC = 1.5 * 2.0 ** 23
FAR = 88.0

CELLS = N * N
COLS = 16
BATCH = COLS * P
KV_GROUPS = [(0, 6), (6, 11), (11, 16)]
MIX_GROUPS = [(0, 4), (4, 8), (8, 12), (12, 16)]
WIDEST = 6
NB = 2 * NT
EROWS = E // P
EPAD = NB * BATCH - E
CELLS_ALL = P * 49152
assert CELLS + BATCH + EPAD <= CELLS_ALL and EPAD == (NB * COLS - EROWS) * P

A0 = 16512
B0 = A0 + 65536
W0 = B0 + NT * GH * ZW * 4
SB_END = 229368


class Own:

    def __init__(self, eng, sem):
        self.eng, self.sem, self.base, self.n = eng, sem, 0, 0

    def mark(self, ins):
        ins.then_inc(self.sem, 1)
        self.n += 1

    def settle(self, but=0):
        after(self.eng, self.sem, self.base + (self.n - but))

    def loop(self, start, end, body):
        n0 = self.n
        body(start)
        base, n1 = self.base, self.n
        per = n1 - n0
        with self.eng.Fori(start + 1, end) as i:
            self.base, self.n = base + n1 + (i - start - 1) * per, 0
            body(i)
            assert self.n == per, (self.n, per)
        self.base, self.n = base, n1 + (end - start - 1) * per


def over_pairs(eng, body, own=None, count=NT):
    body(0, 0)
    n0 = own.n if own else 0
    body(1, 1)
    per = 2 * (own.n - n0) if own else 0
    base, n1 = (own.base, own.n) if own else (0, 0)
    with eng.Fori(1, count // 2 - 1) as i:
        if own:
            own.base, own.n = base + n1 + (i - 1) * per, 0
        body(2 * i, 0)
        body(2 * i + 1, 1)
        assert not own or own.n == per, (own.n, per)
    if own:
        own.base, own.n = base, n1 + (count // 2 - 2) * per
    body(count - 2, 0)
    body(count - 1, 1)


def over_chunks(eng, body, own=None, more=0):
    n0 = own.n if own else 0
    body(0, NC - 1)
    per = own.n - n0 + more if own else 0
    base, n1 = (own.base, own.n) if own else (0, 0)
    with eng.Fori(1, NC - 2) as c:
        if own:
            own.base, own.n = base + n1 + (c - 1) * per, 0
        body(c, 2)
        assert not own or own.n == per, (own.n, per)
    if own:
        own.base, own.n = base, n1 + (NC - 3) * per
    body(NC - 2, 1)
    body(NC - 1, 0)


def over_weight_tiles(eng, body, own=None):
    body(0, 0, None)
    body(1, 1, None)
    for first, last, even in ((1, 1 + GU, True), (1 + GU, 1 + KT, False)):
        base, n1 = (own.base, own.n) if own else (0, 0)
        with eng.Fori(first, last) as i:
            if own:
                own.base, own.n = base + n1 + (i - first) * own.pair[even], 0
            body(2 * i, 0, i - 1 if even else None)
            body(2 * i + 1, 1, i - 1)
            assert not own or own.n == own.pair[even], (own.n, own.pair)
        if own:
            own.base, own.n = base, n1 + (last - first) * own.pair[even]
    body(NT - 2, 0, None)
    body(NT - 1, 1, None)


def known_zero(v):
    return isinstance(v, int) and v <= 0


def after(eng, sem, value):
    if not known_zero(value):
        eng.wait_ge(sem, value)


def apart(eng, sem):
    eng.sem_inc(sem["waits_apart"], 1)


def within(t, n):
    return not isinstance(t, int) or t < n


def build(nc, x, src, dst, w_gat, a_lr, w_qkv_t, w_proj_t, b_proj, clip_x, clip_down, w_gu, w_down, out):
    ctx = ExitStack()
    with ctx:
        cells = nc.dram_tensor("cells", [CELLS_ALL, 1], F32)
        keys_d = nc.dram_tensor("keys_d", [NB * BATCH], F32)
        xt_hi_d = nc.dram_tensor("xt_hi_d", [NT, P, KT * TP], F32)
        xt_lo_d = nc.dram_tensor("xt_lo_d", [NT, P, KT * TP], F32)
        x1_d = nc.dram_tensor("x1_d", [N, D], F32)
        wgu_d = nc.dram_tensor("wgu_d", [GU, P, D], BF16)
        wdn_d = nc.dram_tensor("wdn_d", [KT, P, FIP], BF16)
        sdn_d = nc.dram_tensor("sdn_d", [D, 1], F32)

        def at(name, offset, shape, dt):
            size = BYTES[dt]
            for s in shape[1:]:
                size *= s
            assert offset % 32 == 0 and offset + size <= SB_END, (name, offset + size)
            return nc.alloc_sbuf_tensor_at(name, shape, dt, offset=offset)

        class Row:

            def __init__(self, start, end):
                self.at, self.end = start, end

            def put(self, name, shape, dt):
                t = at(name, self.at, shape, dt)
                size = BYTES[dt]
                for s in shape[1:]:
                    size *= s
                self.at += (size + 31) // 32 * 32
                assert self.at <= self.end + 31, (name, self.at - self.end)
                return t

        A_raw = at("A_raw", A0 + 32768, [P, KT, D], F32)
        A_hi = at("A_hi", A0, [P, KT, D], F32R)
        A_lo = at("A_lo", A0 + 32768, [P, KT, D], F32R)
        B_raw = at("B_raw", B0 + 32768, [P, KT, D], F32)
        B_hi = at("B_hi", B0, [P, KT, D], F32R)
        B_lo = at("B_lo", B0 + 32768, [P, KT, D], F32R)
        tail = B0 + 65536
        keyrow = at("keyrow", tail, [P, 2, BATCH], F32)
        src_i = at("src_i", tail, [TP, 640], I32)
        dst_i = at("dst_i", tail + 2560, [TP, 640], I32)
        key_f = at("key_f", tail + 5120, [TP, 640], F32)
        pad_i = at("pad_i", tail + 7680, [15, P], I32)
        pad_f = at("pad_f", tail + 8192, [15, P], F32)
        dummy_i = at("dummy_i", tail + 8704, [P, COLS], I32)
        z = at("z", B0, [TP, NT, GH, ZW], F32)

        w = Row(W0, SB_END)
        ident = w.put("ident", [P, P], F32)
        ident_b = w.put("ident_b", [P, P], BF16)
        ones = w.put("ones", [P, P], F32)
        elr = w.put("elr", [TP, NT, 8], F32)
        el02 = w.put("el02", [TP, NT, GH], F32)
        stats = w.put("stats", [TP, 2, 6], F32)
        mv = w.put("mv", [TP, 2, 2], F32)
        rst = w.put("rst", [TP, 2, 4], F32)
        tiny = w.put("tiny", [P, 64], F32)
        far = w.put("far", [P, 1], F32)
        wscale = w.put("wscale", [P, GU + KT], F32)
        wsc = w.put("wsc", [P, 2], F32)
        mv2 = w.put("mv2", [TP, NT, 2], F32)
        work = w.at

        w = Row(work, SB_END)
        first_w = w.put("first_w", [P, (2 * WIDEST - 1) * P], BF16)
        keycol = w.put("keycol", [P, NB * COLS], F32)
        count = w.put("count", [P, NB * COLS], F32)
        cell = at("cell", w.at - 2 * NB * COLS * 4, [P, NB * COLS], U32)
        cell_now = w.put("cell_now", [P, COLS], U32)
        count_now = w.put("count_now", [P, COLS], F32)
        own_cell = w.put("own_cell", [P, COLS], F32)
        is_first = w.put("is_first", [P, COLS], F32)
        key_off = w.put("key_off", [P, COLS], F32)
        junk = w.put("junk", [P, 2, WIDEST * P], BF16)
        zero = w.put("zero", [P, P], F32)
        xbuf = w.put("xbuf", [TP, 2, D], F32)
        xh = w.put("xh", [P, 2, KT * TP], F32R)
        xl = w.put("xl", [P, 2, KT * TP], F32R)
        slot = w.at
        w = Row(slot, SB_END)
        xn = w.put("xn", [TP, D], F32)
        ebuf = w.put("ebuf", [TP, 2, D], F32)
        vbuf = w.put("vbuf", [TP, 2, D], F32)
        ksum = w.put("ksum", [TP, D], F32)
        assert w.at - slot == 6 * 4096
        w = Row(slot, SB_END)
        bias_b = w.put("bias_b", [TP, D], F32)
        qbuf = w.put("qbuf", [TP, D], F32)
        qk = w.put("qk", [TP, D], F32)
        q_hi = at("q_hi", w.at, [P, KT * TP], F32R)
        kvT = w.put("kvT", [P, KT, P], F32)
        ksum_b = w.put("ksum_b", [TP, D], F32)
        q_lo = w.put("q_lo", [P, KT * TP], F32R)
        a_b = at("a_b", slot + 4096, [TP, 2, D], F32)
        w = Row(slot + 12288, SB_END)
        wrow = w.put("wrow", [P, 2, D], F32)
        wint = at("wint", slot, [P, 2, D], BF16)
        wturn = at("wturn", slot + 12288 + 8192, [P, 2, D], BF16)

        g = Row(A0, B0)
        cnt_c = g.put("cnt_c", [TP, NT, CW], F32)
        e1 = g.put("e1", [TP, 4, CW], F32)
        e2 = g.put("e2", [TP, 4, CW], F32)
        diag = g.put("diag", [TP, 2, JT, TP], F32)
        no_edge = g.put("no_edge", [TP, 2, CW], F32)
        g = Row(work, SB_END)
        rb = g.put("rb", [TP, 2, 8, CW], F32)
        nmin = g.put("nmin", [TP, GH, CW], F32)
        cnt_m = g.put("cnt_m", [TP, 2, CW], F32)
        prob = g.put("prob", [TP, 4, CW], F32)
        x1c = g.put("x1c", [TP, 2, JT, GF], F32)
        rr = g.put("rr", [TP, 8, JT], F32)
        st2 = g.put("st2", [TP, JT, GH, 6], F32)
        mvc = g.put("mvc", [TP, JT, 2], F32)

        xn2 = at("xn2", B0, [TP, NT, D], F32)
        f = Row(A0, B0)
        wguT = f.put("wguT", [P, GU, KT, P], BF16)
        wdnT = f.put("wdnT", [P, KT, 3, P], BF16)
        sdb = f.put("sdb", [TP, D], F32)
        xqT = f.put("xqT", [P, 2, KT, CW], BF16)
        xrnd = f.put("xrnd", [TP, 2, D], F32)
        xint = f.put("xint", [TP, 2, D], BF16)
        y = f.put("y", [TP, 2, D], F32)
        amax = f.put("amax", [P, NT], F32)
        rs2 = f.put("rs2", [TP, 4, NT], F32)
        f = Row(work, SB_END)
        hT = f.put("hT", [P, 3, N], F32)
        hqT = f.put("hqT", [P, 3, N], BF16)
        gsil = f.put("gsil", [P, 3, CW], F32)

        ps = ctx.enter_context(nc.psum_tensor("ps", [P, 8, HALF], F32))

        def banks(b, n, rows=P):
            return ps[0:rows, b:b + n, :].rearrange("p b c -> p (b c)")

        SEMS = """wrow_loaded0 wrow_loaded1 wint_ready0 wint_ready1 wT_done0 wT_done1 wT_ready0 wT_ready1 wT_stored0
        wT_stored1 wpad_zero scales_ready scales_stored w2_loaded x1t_loaded0 x1t_loaded1 x1t_loaded2
        x1t_loaded3 xr_loaded0 xr_loaded1 stats_ready rstd_ready waits_apart far_set ind_ready zero_ready
        consts_ready edges_loaded key_ready keysT_done keycol_ready keys_stored cells_zeroed keyrow_loaded0
        keyrow_loaded1 counted cell_ready pool_own dve_own clip_free pads_zero xmax_ready hmax_ready
        now_ready scattered x_loaded0 x_loaded1 var_ready act_own r0_ready xn_ready xnT_done hi_ready
        lo_ready xt_stored0 xt_stored1 w_hi_ready w_lo_ready k_done v_done kv_done exp_ready kmin_ready
        k_ready v_ready ksum_done ksumb_done ksumb_ready kvT_zero kvT_ready xt_loaded0 xt_loaded1 x2_loaded0
        x2_loaded1 bias_loaded q_done q_ready qs_ready qT_done qhi_ready qlo_ready g_done ghi_ready glo_ready
        mix_done xb_ready x1_ready x1_stored0 x1_stored1 a_loaded z_done z_ready z_ones el_ready el02_ready
        cm_loaded nmax_ready nmaxT_done rr_ready diag_ready bc_done rb_ready cc_loaded0 cc_loaded1 cc_loaded2
        cc_loaded3 e_ready emax_ready p_ready p_used x1c_loaded0 x1c_loaded1 x1c_ready x1c_stored0
        x1c_stored1 xn2_ready mxT_done mxs_ready mxb_done scale_ready clip_loaded sig_ready rnd_ready
        xint_ready xqT_done xqT_ready gu_done sil_ready h_ready hmxT_done hmxs_ready hmxb_done hscale_ready
        hrnd_ready hq_ready down_done y_ready out_ready0 out_ready1 out_stored0 out_stored1""".split()
        sem = {name: ctx.enter_context(nc.semaphore(name)) for name in SEMS}
        slab_a = [ctx.enter_context(nc.semaphore(f"slab_a{i}")) for i in range(KT)]
        slab_b = [ctx.enter_context(nc.semaphore(f"slab_b{i}")) for i in range(KT)]
        x_loaded = [sem["x_loaded0"], sem["x_loaded1"]]
        keyrow_loaded = [sem["keyrow_loaded0"], sem["keyrow_loaded1"]]
        xt_stored = [sem["xt_stored0"], sem["xt_stored1"]]
        xt_loaded = [sem["xt_loaded0"], sem["xt_loaded1"]]
        x2_loaded = [sem["x2_loaded0"], sem["x2_loaded1"]]
        x1_stored = [sem["x1_stored0"], sem["x1_stored1"]]
        cc_loaded = [sem[f"cc_loaded{i}"] for i in range(4)]
        x1c_loaded = [sem["x1c_loaded0"], sem["x1c_loaded1"]]
        x1c_stored = [sem["x1c_stored0"], sem["x1c_stored1"]]
        wrow_loaded = [sem["wrow_loaded0"], sem["wrow_loaded1"]]
        wint_ready = [sem["wint_ready0"], sem["wint_ready1"]]
        wT_done = [sem["wT_done0"], sem["wT_done1"]]
        wT_ready = [sem["wT_ready0"], sem["wT_ready1"]]
        wT_stored = [sem["wT_stored0"], sem["wT_stored1"]]
        x1t_loaded = [sem[f"x1t_loaded{i}"] for i in range(4)]
        xr_loaded = [sem["xr_loaded0"], sem["xr_loaded1"]]
        out_ready = [sem["out_ready0"], sem["out_ready1"]]
        out_stored = [sem["out_stored0"], sem["out_stored1"]]

        def half_of(t):
            return 16 * (t // 2 + 1)

        def cells_tile(t, c):
            m = cells.ap()[0:CELLS, :].rearrange("(m n) o -> m (n o)", n=N)
            return m[bass.ds(t * TP, TP), bass.ds(c * CW, CW)]

        def weights_stored(eng):
            for par in range(2):
                eng.wait_ge(wrow_loaded[par], 16 * ((GU, KT)[par] + 1))
                eng.wait_ge(wT_stored[par], 16 * ((GU, KT)[par] + 1))

        block = ctx.enter_context(nc.Block())

        @block.sync
        def _(sp):
            def rows(t):
                return x[bass.ds(t * TP, TP), :]

            def load_x(t, par):
                sp.dma_start(xbuf[:, par, :], rows(t)).then_inc(x_loaded[par], 16)

            load_x(0, 0)
            load_x(1, 1)
            sp.dma_start(src_i[:], src.rearrange("(p c) -> p c", p=TP)).then_inc(sem["edges_loaded"], 16)
            sp.dma_start(dst_i[:], dst.rearrange("(p c) -> p c", p=TP)).then_inc(sem["edges_loaded"], 16)
            for kt in range(KT):
                sp.dma_start(A_raw[:, kt, :], w_qkv_t[kt * P:(kt + 1) * P, D:2 * D]).then_inc(slab_a[kt], 16)
            sp.wait_ge(sem["key_ready"], 2)
            sp.dma_start(keys_d.ap()[0:E].rearrange("(p c) -> p c", p=TP), key_f[:]).then_inc(sem["keys_stored"], 16)
            sp.dma_start(keys_d.ap()[E:NB * BATCH].rearrange("(p c) -> p c", p=15), pad_f[:]).then_inc(sem["keys_stored"], 16)
            for kt in range(KT):
                sp.dma_start(B_raw[:, kt, :], w_qkv_t[kt * P:(kt + 1) * P, 2 * D:3 * D]).then_inc(slab_b[kt], 16)
            sp.wait_ge(sem["keys_stored"], 32)
            sp.wait_ge(sem["keysT_done"], 1)
            sp.wait_ge(sem["key_ready"], 3)

            def load_keys(b, par):
                sp.dma_start(keyrow[:, par, :], keys_d.ap()[bass.ds(b * BATCH, BATCH)].unsqueeze(0).to_broadcast([P, BATCH]))\
                  .then_inc(keyrow_loaded[par], 16)

            load_keys(0, 0)
            load_keys(1, 1)

            def store_xt(t, par):
                sp.wait_ge(sem["lo_ready"], t + 1)
                sp.dma_start(xt_hi_d.ap()[bass.ds(t, 1), :, :].rearrange("o p c -> (o p) c"), xh[:, par, :].bitcast(F32)).then_inc(xt_stored[par], 16)
                sp.dma_start(xt_lo_d.ap()[bass.ds(t, 1), :, :].rearrange("o p c -> (o p) c"), xl[:, par, :].bitcast(F32)).then_inc(xt_stored[par], 16)

            store_xt(0, 0)

            def load_xt(t, par):
                sp.dma_start(xh[:, par, :].bitcast(F32), xt_hi_d.ap()[bass.ds(t, 1), :, :].rearrange("o p c -> (o p) c")).then_inc(xt_loaded[par], 16)
                sp.dma_start(xl[:, par, :].bitcast(F32), xt_lo_d.ap()[bass.ds(t, 1), :, :].rearrange("o p c -> (o p) c")).then_inc(xt_loaded[par], 16)

            def load_x2(t, par):
                sp.dma_start(xbuf[:, par, :], rows(t)).then_inc(x2_loaded[par], 16)

            def start_mix():
                sp.wait_ge(sem["k_done"], NT)
                for kt in range(KT):
                    sp.dma_start(A_raw[:, kt, :], w_qkv_t[kt * P:(kt + 1) * P, 0:D]).then_inc(slab_a[kt], 16)
                for par in range(2):
                    sp.wait_ge(xt_stored[par], 32 * NT // 2)
                sp.wait_ge(sem["v_done"], NT - 1)
                load_xt(0, 0)
                load_x2(0, 0)
                load_x2(1, 1)
                sp.wait_ge(sem["v_done"], NT)
                for kt in range(KT):
                    sp.dma_start(B_raw[:, kt, :], w_proj_t[kt * P:(kt + 1) * P, :]).then_inc(slab_b[kt], 16)
                load_xt(1, 1)
                sp.dma_start(bias_b[:], b_proj.unsqueeze(0).to_broadcast([TP, D])).then_inc(sem["bias_loaded"], 16)

            def kv_tile(t, par):
                if within(t, NT - 2):
                    sp.wait_ge(sem["xn_ready"], t + 1)
                    load_x(t + 2, par)
                if within(t, NT - 1):
                    store_xt(t + 1, 1 - par)
                if not within(t, NT - 1):
                    start_mix()
                sp.wait_ge(sem["counted"], t + 1)
                load_keys(t + 2, par)

            over_pairs(sp, kv_tile)

            def mix_tile(t, par):
                if within(t, NT - 2):
                    sp.wait_ge(sem["q_done"], t + 1)
                    load_xt(t + 2, par)
                if within(t, NT - 2):
                    sp.wait_ge(sem["counted"], NT + t + 1)
                    load_keys(NT + t + 2, par)
                sp.wait_ge(sem["x1_ready"], t + 1)
                sp.dma_start(x1_d.ap()[bass.ds(t * TP, TP), :], xbuf[:, par, :]).then_inc(x1_stored[par], 16)
                if within(t, NT - 2):
                    sp.wait_ge(x1_stored[par], half_of(t))
                    load_x2(t + 2, par)
                if isinstance(t, int) and t == NT - 2:
                    sp.wait_ge(sem["q_done"], NT)
                    for kt in range(KT):
                        sp.dma_start(A_raw[:, kt, :], w_gat[kt * P:(kt + 1) * P, :]).then_inc(slab_a[kt], 16)
                    load_xt(0, 0)
                    load_xt(1, 1)

            over_pairs(sp, mix_tile)
            sp.wait_ge(sem["qT_done"], NT)
            sp.wait_ge(sem["qs_ready"], NT)
            sp.wait_ge(sem["q_done"], NT)
            sp.dma_start(a_b[:], a_lr.unsqueeze(0).to_broadcast([TP, 2, D])).then_inc(sem["a_loaded"], 16)

            sp.wait_ge(sem["mix_done"], NT)

            def load_gu(b):
                sp.dma_start(wrow[:, 0, :], w_gu[bass.ds(b * P, P), :]).then_inc(wrow_loaded[0], 16)

            def load_dn(b):
                sp.dma_start(wrow[:, 1, 0:FI], w_down[bass.ds(b * P, P), :]).then_inc(wrow_loaded[1], 16)

            def store_turned(par, b):
                if par == 0:
                    sp.dma_start(wgu_d.ap()[bass.ds(b, 1), :, :].rearrange("o p c -> (o p) c"), wturn[:, 0, :]).then_inc(wT_stored[0], 16)
                else:
                    sp.dma_start(wdn_d.ap()[bass.ds(b, 1), :, :].rearrange("o p c -> (o p) c"), wturn[:, 1, 0:FIP]).then_inc(wT_stored[1], 16)

            load_gu(0)
            load_dn(0)
            for par in range(2):
                sp.sem_inc(wT_stored[par], 16)

            def z_tile(t, par, b):
                if within(t, NT - 2):
                    sp.wait_ge(sem["z_done"], t + 1)
                    load_xt(t + 2, par)
                if b is None:
                    return
                sp.wait_ge(wT_ready[par], b + 2)
                store_turned(par, b)
                if par == 0:
                    load_gu((b + 1) % GU)
                else:
                    load_dn((b + 1) % KT)

            over_weight_tiles(sp, z_tile)

            sp.wait_ge(sem["scattered"], 16 * NB * COLS)
            sp.wait_ge(sem["z_done"], NT)

            def load_counts(t, c, s):
                sp.dma_start(cnt_c[:, bass.ds(t, 1), :].rearrange("p o c -> p (o c)"), cells_tile(t, c)).then_inc(cc_loaded[s], 16)

            def first_chunk(i):
                for s in range(4):
                    after(sp, cc_loaded[s], 16 * i)
                    load_counts(4 * i + s, 0, s)

            first_chunk(0)
            with sp.Fori(1, NT // 4) as i:
                first_chunk(i)
            sp.wait_ge(sem["scales_ready"], 1)
            for b in range(KT):
                sp.dma_start(sdn_d.ap()[b * P:(b + 1) * P, :], wscale[:, GU + b:GU + b + 1]).then_inc(sem["scales_stored"], 16)
            weights_stored(sp)
            sp.wait_ge(sem["scales_stored"], 16 * KT)
            sp.wait_ge(sem["el_ready"], NT)

            def load_counts_for_max(m):
                if not (isinstance(m, int) and m < NT + 2):
                    sp.wait_ge(sem["ind_ready"], m - 1)
                after(sp, sem["cm_loaded"], 16 * (m - NT))
                sp.dma_start(cnt_m[:, bass.ds(m % 2, 1), :].rearrange("p o c -> p (o c)"), cells_tile(m % NT, m // NT))\
                  .then_inc(sem["cm_loaded"], 16)

            for m in range(NT, NT + 6):
                load_counts_for_max(m)

            def gat_chunk(c, left):
                for h in range(GH):
                    live = left >= (1 if h < 3 else 2)
                    count = 4 if left == 1 and h == 2 else 5
                    if live or (h == 3 and left):
                        with sp.Fori(0, count) as u:
                            if live:
                                load_counts_for_max((4 * c + h) * 5 + u + 26)
                            if h == 3:
                                for s in range(4):
                                    sp.wait_ge(sem["p_ready"], ((4 * c + 3) * 5 + u) * 2 + s // 2 + 1)
                                    load_counts(4 * u + s, c + 1, s)
                                for s in range(4):
                                    sp.wait_ge(cc_loaded[s], 16 * ((c + 1) * 5 + u + 1))
                                apart(sp, sem)

            over_chunks(sp, gat_chunk)

            def x1_tile(t):
                return x1_d.ap()[bass.ds(t * TP, TP), :]

            def slot_of(t):
                return xn2[:, bass.ds(t, 1), :].rearrange("p o d -> p (o d)")

            def load_x1(i, last_head=True):
                for s in range(4):
                    if last_head:
                        sp.wait_ge(sem["p_used"], NT * (GH * NC - 1) + 4 * i + s + 1)
                        apart(sp, sem)
                    after(sp, x1t_loaded[s], 16 * i)
                    sp.dma_start(slot_of(4 * i + s), x1_tile(4 * i + s)).then_inc(x1t_loaded[s], 16)

            def stored(chunks):
                for par in range(2):
                    sp.wait_ge(x1c_stored[par], 16 * chunks * GH // 2)

            stored(NC - 1)
            load_x1(0)
            with sp.Fori(1, NC - 1) as i:
                load_x1(i)
            sp.wait_ge(sem["p_used"], GH * NC * NT)
            stored(NC)
            load_x1(NC - 1, last_head=False)
            sp.wait_ge(sem["clip_free"], 1)
            sp.dma_start(tiny[:, 40:41], clip_x.unsqueeze(0).to_broadcast([P, 1])).then_inc(sem["clip_loaded"], 16)
            sp.dma_start(tiny[:, 41:42], clip_down.unsqueeze(0).to_broadcast([P, 1])).then_inc(sem["clip_loaded"], 16)
            sp.dma_start(wguT[:].rearrange("p b k c -> p b (k c)"), wgu_d.ap().rearrange("b p c -> p b c")).then_inc(sem["w2_loaded"], 16)
            sp.dma_start(wdnT[:].rearrange("p b i c -> p b (i c)"), wdn_d.ap().rearrange("b p c -> p b c")).then_inc(sem["w2_loaded"], 16)
            sp.dma_start(sdb[:], sdn_d.ap().rearrange("n o -> o n").to_broadcast([TP, D])).then_inc(sem["w2_loaded"], 16)

            def residual(t, par):
                sp.wait_ge(sem["rnd_ready"], t + 1)
                if not (isinstance(t, int) and t < 2):
                    sp.wait_ge(xr_loaded[par], 16 * (t // 2))
                sp.dma_start(slot_of(t), x1_tile(t)).then_inc(xr_loaded[par], 16)

            over_pairs(sp, residual)

            def out_tile(t, par):
                sp.wait_ge(out_ready[par], t // 2 + 1)
                sp.dma_start(out[bass.ds(t * TP, TP), :], slot_of(t)).then_inc(out_stored[par], 16)

            over_pairs(sp, out_tile)
            for par in range(2):
                sp.wait_ge(out_stored[par], 16 * NT // 2)

        @block.gpsimd
        def _(pool):
            pool.memset(zero[:], 0.0).then_inc(sem["zero_ready"], 1)
            pool.memset(ident[:], 0.0).then_inc(sem["pool_own"], 1)
            pool.memset(ones[:], 1.0).then_inc(sem["pool_own"], 1)
            pool.memset(far[:], FAR).then_inc(sem["far_set"], 1)
            pool.memset(first_w[:], 1.0).then_inc(sem["pool_own"], 1)
            pool.iota(pad_i[:], pattern=[[1, P]], base=CELLS + BATCH, channel_multiplier=P).then_inc(sem["consts_ready"], 1)
            pool.iota(dummy_i[:], pattern=[[P, COLS]], base=CELLS, channel_multiplier=1).then_inc(sem["consts_ready"], 1)
            pool.wait_ge(sem["pool_own"], 3)
            pool.affine_select(out=ident[:], in_=ident[:], compare_op=ALU.not_equal, fill=1.0, base=0,
                               pattern=[[-1, P]], channel_multiplier=1).then_inc(sem["consts_ready"], 1)
            pool.affine_select(out=first_w[:], in_=first_w[:], compare_op=ALU.is_ge, fill=1024.0, base=-(WIDEST - 1) * P,
                               pattern=[[1, (2 * WIDEST - 1) * P]], channel_multiplier=-1).then_inc(sem["consts_ready"], 1)
            pool.wait_ge(sem["consts_ready"], 3)
            pool.tensor_copy(ident_b[:], ident[:]).then_inc(sem["consts_ready"], 1)

            pool.wait_ge(sem["cells_zeroed"], 16 * 12)

            def add_batch(b, groups):
                pool.wait_ge(sem["cell_ready"], b + 1)
                pool.tensor_copy(cell_now[:], cell[:, bass.ds(b * COLS, COLS)]).then_inc(sem["now_ready"], 1)
                pool.tensor_copy(count_now[:], count[:, bass.ds(b * COLS, COLS)]).then_inc(sem["now_ready"], 1)
                pool.wait_ge(sem["now_ready"], 2 * b + 2)
                apart(pool, sem)
                for first, end in groups:
                    for q in range(first, end):
                        pool.indirect_dma_start(out=cells.ap(), out_offset=bass.IndirectOffsetOnAxis(cell_now[:, q:q + 1], 0),
                                                in_=count_now[:, q:q + 1], in_offset=None, compute_op=ALU.add)\
                            .then_inc(sem["scattered"], 16)
                    pool.wait_ge(sem["scattered"], 16 * (b * COLS + end))
                    apart(pool, sem)

            with pool.Fori(0, NT) as b:
                add_batch(b, KV_GROUPS)
            with pool.Fori(NT, NB) as b:
                add_batch(b, MIX_GROUPS)

            for par in range(2):
                pool.wait_ge(x1_stored[par], 16 * NT // 2)
            pool.wait_ge(sem["z_done"], NT)
            pool.wait_ge(sem["el_ready"], NT)

            def head_rows(c, h):
                return x1_d.ap()[bass.ds(c * CW, CW), h * GF:(h + 1) * GF].rearrange("(j p) f -> p j f", p=TP)

            def load_x1c(c, h):
                pool.dma_start(x1c[:, h % 2, :, :], head_rows(c, h)).then_inc(x1c_loaded[h % 2], 16)

            def diagonals(c):
                for r in range(8):
                    pool.wait_ge(sem["rr_ready"], c + 1)
                    after(pool, sem["bc_done"], 8 * c + r - 1)
                    pool.tensor_tensor(diag[:, r % 2, :, :], ident[0:TP, 0:TP].unsqueeze(1).to_broadcast([TP, JT, TP]),
                                       rr[:, r, :].unsqueeze(2).to_broadcast([TP, JT, TP]), ALU.mult).then_inc(sem["diag_ready"], 1)

            weights_stored(pool)
            load_x1c(0, 0)
            load_x1c(0, 1)
            diagonals(0)

            def gat_chunk(c, left):
                for h in range(GH):
                    if h == 3 and left:
                        diagonals(c + 1)
                    pool.wait_ge(sem["x1c_ready"], 4 * c + h + 1)
                    apart(pool, sem)
                    pool.dma_start(head_rows(c, h), x1c[:, h % 2, :, :]).then_inc(x1c_stored[h % 2], 16)
                    if h < 2 or left:
                        pool.wait_ge(x1c_stored[h % 2], 16 * (2 * c + h // 2 + 1))
                        apart(pool, sem)
                        load_x1c(c + h // 2, (h + 2) % 4)

            over_chunks(pool, gat_chunk)

            pool.wait_ge(sem["p_used"], GH * NC * NT)
            pool.wait_ge(x1c_stored[0], 16 * NC * GH // 2)
            pool.wait_ge(x1c_stored[1], 16 * NC * GH // 2)
            pool.wait_ge(sem["x1c_ready"], GH * NC)
            pool.memset(hT[:, 2, :], 0.0).then_inc(sem["pads_zero"], 1)

            def out_tile(t, par):
                if par:
                    return
                pool.wait_ge(sem["y_ready"], t + 1)
                pool.wait_ge(xr_loaded[par], half_of(t))
                xt = xn2[:, bass.ds(t, 1), :].rearrange("p o d -> p (o d)")
                pool.tensor_tensor(xt, xt, y[:, par, :], ALU.add).then_inc(out_ready[par], 1)

            over_pairs(pool, out_tile)

        @block.tensor
        def _(pe):
            def project(bank, hi, lo, w_hi, w_lo, ready=None):
                for kt in range(KT):
                    if ready:
                        pe.wait_ge(ready[0], ready[1] + kt + 1)
                    cols = slice(kt * TP, (kt + 1) * TP)
                    for n, (a, wt) in enumerate(((hi, w_hi), (hi, w_lo), (lo, w_hi))):
                        for half in range(2):
                            last = pe.matmul(ps[0:TP, bank + half, :], a[:, cols], wt[:, kt, half * HALF:(half + 1) * HALF],
                                             start=kt == 0 and n == 0, stop=kt == KT - 1 and n == 2)
                return last

            def turn(source):
                for kt in range(KT):
                    last = pe.transpose(ps[:, 6 + kt // 4, (kt % 4) * TP:(kt % 4 + 1) * TP], source[:, kt * P:(kt + 1) * P],
                                        ident[0:TP, 0:TP])
                return last

            pe.wait_ge(sem["consts_ready"], 3)
            pe.wait_ge(sem["key_ready"], 2)
            for a in range(5):
                pe.transpose(ps[:, 4 + a // 4, (a % 4) * TP:(a % 4 + 1) * TP], key_f[:, a * P:(a + 1) * P], ident[0:TP, 0:TP])
            pe.transpose(ps[:, 5, TP:TP + 15], pad_f[:], ident[0:15, 0:15]).then_inc(sem["keysT_done"], 1)

            def turn_x(t):
                pe.wait_ge(sem["xn_ready"], t + 1)
                turn(xn).then_inc(sem["xnT_done"], 1)

            def kv(t, par):
                for p in range(KT):
                    last = pe.matmul(ps[:, 4 + p // 4, (p % 4) * P:(p % 4 + 1) * P], vbuf[:, par, p * P:(p + 1) * P],
                                     ebuf[:, par, p * P:(p + 1) * P], start=isinstance(t, int) and t == 0 and p % 4 == 0,
                                     stop=isinstance(t, int) and t == NT - 1, skip_group_check=True)
                last.then_inc(sem["kv_done"], 1)

            turn_x(0)

            def kv_tile(t, par):
                first = isinstance(t, int) and t == 0
                pe.wait_ge(sem["lo_ready"], t + 1)
                after(pe, sem["k_ready"], t)
                project(0, xh[:, par, :], xl[:, par, :], A_hi, A_lo, (sem["w_lo_ready"], 0) if first else None)\
                    .then_inc(sem["k_done"], 1)
                if within(t, NT - 1):
                    turn_x(t + 1)
                after(pe, sem["v_ready"], t)
                if first:
                    pe.wait_ge(sem["keycol_ready"], 1)
                else:
                    kv(t - 1, 1 - par)
                project(2, xh[:, par, :], xl[:, par, :], B_hi, B_lo, (sem["w_lo_ready"], KT) if first else None)\
                    .then_inc(sem["v_done"], 1)

            def queries(t, par):
                first = isinstance(t, int) and t == 0
                pe.wait_ge(xt_loaded[par], 2 * half_of(t))
                if not first:
                    pe.wait_ge(sem["q_ready"], t)
                project(0, xh[:, par, :], xl[:, par, :], A_hi, A_lo, (sem["w_lo_ready"], 2 * KT) if first else None)\
                    .then_inc(sem["q_done"], 1)

            over_pairs(pe, kv_tile)
            pe.wait_ge(sem["k_ready"], NT)
            queries(0, 0)
            pe.wait_ge(sem["v_ready"], NT)
            kv(NT - 1, 1)
            pe.wait_ge(sem["ksum_done"], NT + 1)
            for half in range(2):
                last = pe.matmul(ps[0:TP, 2 + half, :], ones[0:TP, 0:TP], ksum[:, half * HALF:(half + 1) * HALF], start=True, stop=True)
            last.then_inc(sem["ksumb_done"], 1)

            def turn_q(t):
                pe.wait_ge(sem["qs_ready"], t + 1)
                turn(qbuf).then_inc(sem["qT_done"], 1)

            pe.wait_ge(sem["kvT_ready"], 2)
            for p in range(KT):
                bank = 6 if p % 2 == 0 else 4
                pe.wait_ge(slab_b[p], 32)
                after(pe, sem["glo_ready"], p - 1)
                for half in range(2):
                    last = pe.matmul(ps[:, bank + half, :], kvT[:, p, :], B_raw[:, p, half * HALF:(half + 1) * HALF],
                                     start=True, stop=True)
                last.then_inc(sem["g_done"], 1)
            pe.wait_ge(sem["glo_ready"], KT)
            turn_q(0)

            def mix_tile(t, par):
                if within(t, NT - 1):
                    queries(t + 1, 1 - par)
                pe.wait_ge(sem["qlo_ready"], t + 1)
                if isinstance(t, int) and t == 0:
                    pe.wait_ge(sem["ksumb_ready"], 1)
                else:
                    pe.wait_ge(sem["x1_ready"], t)
                project(2, q_hi, q_lo, B_hi, B_lo).then_inc(sem["mix_done"], 1)
                if within(t, NT - 1):
                    turn_q(t + 1)

            over_pairs(pe, mix_tile)

            def bank_b(b, rows=P):
                return ps[0:rows, b, :].bitcast(BF16)

            def z_tile(t, par, b):
                first = isinstance(t, int) and t == 0
                pe.wait_ge(xt_loaded[par], 16 * NT + 2 * half_of(t))
                if isinstance(t, int) and t < 2:
                    pe.wait_ge(sem["q_ready"] if t == 0 else sem["x1_ready"], NT)
                else:
                    pe.wait_ge(sem["z_ready"], t - 1)
                project(2 * par, xh[:, par, :], xl[:, par, :], A_hi, A_lo, (sem["w_lo_ready"], 3 * KT) if first else None)\
                    .then_inc(sem["z_done"], 1)
                if b is None:
                    return
                pe.wait_ge(wint_ready[par], b + 1)
                pe.wait_ge(wT_ready[par], b + 1)
                for i, (c0, cn) in enumerate([(i * P, P) for i in range(KT)] if par == 0 else IB):
                    last = pe.transpose(bank_b(6 + par, cn)[:, i * P:(i + 1) * P], wint[:, par, c0:c0 + cn], ident_b[:, :])
                last.then_inc(wT_done[par], 1)

            pe.wait_ge(sem["consts_ready"], 5)
            for par in range(2):
                pe.sem_inc(wT_done[par], 1)
            over_weight_tiles(pe, z_tile)

            def turn_maxima(c):
                pe.wait_ge(sem["nmax_ready"], NT * (c + 1))
                for j in range(JT):
                    for h in range(GH):
                        last = pe.transpose(ps[0:TP, j, h * TP:(h + 1) * TP], nmin[:, h, j * TP:(j + 1) * TP], ident[0:TP, 0:TP])
                last.then_inc(sem["nmaxT_done"], 1)

            def spread(c, r):
                pe.wait_ge(sem["diag_ready"], 8 * c + r + 1)
                if r >= 4:
                    pe.wait_ge(sem["rb_ready"], 8 * c + r - 3)
                pe.matmul(ps[0:TP, r % 4, 0:CW], ones[0:TP, 0:TP], diag[:, r % 2, :, :].rearrange("p j q -> p (j q)"),
                          start=True, stop=True).then_inc(sem["bc_done"], 1)

            def gat_steps(c, h, u):
                for s in range(4):
                    if s % 2 == 0:
                        pe.wait_ge(sem["p_ready"], ((4 * c + h) * 5 + u) * 2 + s // 2 + 1)
                    for j in range(JT):
                        last = pe.matmul(ps[0:TP, 4 * (h % 2) + j, 0:ZW], prob[:, s, j * TP:(j + 1) * TP],
                                         z[:, bass.ds(4 * u + s, 1), h, :].rearrange("p o f -> p (o f)"),
                                         start=isinstance(u, int) and u == 0 and s == 0,
                                         stop=isinstance(u, int) and u == 4 and s == 3)
                    last.then_inc(sem["p_used"], 1)

            pe.wait_ge(sem["z_ready"], NT)
            pe.wait_ge(sem["z_ones"], 1)
            turn_maxima(0)
            pe.wait_ge(sem["rr_ready"], 1)
            for r in range(8):
                spread(0, r)
            pe.wait_ge(sem["rb_ready"], 8)

            def gat_chunk(c, left):
                for h in range(GH):
                    after(pe, sem["x1c_ready"], 4 * c + h - 1)
                    gat_steps(c, h, 0)
                    if h == 3 and left:
                        pe.wait_ge(sem["x1c_ready"], 4 * c + 3)
                        turn_maxima(c + 1)
                        gat_steps(c, h, 1)
                        gat_steps(c, h, 2)
                        pe.wait_ge(sem["rr_ready"], c + 2)
                        for r in range(4):
                            spread(c + 1, r)
                        gat_steps(c, h, 3)
                        for r in range(4, 8):
                            spread(c + 1, r)
                    else:
                        with pe.Fori(1, 4) as u:
                            gat_steps(c, h, u)
                    gat_steps(c, h, 4)

            over_chunks(pe, gat_chunk)

            def spread_max(col, ready, turned, m_ready, done, bank):
                pe.wait_ge(ready, 1)
                pe.transpose(ps[0:1, bank, 0:P], tiny[:, col:col + 1], ident[:, :]).then_inc(turned, 1)
                pe.wait_ge(m_ready, 1)
                pe.matmul(ps[:, bank, P:P + 1], ones[0:1, :], tiny[0:1, col + 1:col + 2], start=True, stop=True)\
                    .then_inc(done, 1)

            spread_max(42, sem["xmax_ready"], sem["mxT_done"], sem["mxs_ready"], sem["mxb_done"], 0)

            def turn_tile(c, j):
                t = 4 * c + j
                pe.wait_ge(sem["xint_ready"], t + 1)
                after(pe, sem["xqT_ready"], t - 1)
                for kt in range(KT):
                    last = pe.transpose(bank_b(6 + j % 2)[:, kt * P:kt * P + TP], xint[:, j % 2, kt * P:(kt + 1) * P], ident_b[0:TP, 0:TP])
                last.then_inc(sem["xqT_done"], 1)

            def gate_up(c, i):
                i0, rows_n = IB[i]
                if i == 0:
                    pe.wait_ge(sem["xqT_ready"], JT * (c + 1))
                after(pe, sem["h_ready"], 3 * (c - 1) + i + 1)
                for g in range(2):
                    for kt in range(KT):
                        last = pe.matmul(ps[0:rows_n, 2 * i + g, 0:CW], wguT[:, 3 * g + i, kt, 0:rows_n],
                                         xqT[:, bass.ds(c % 2, 1), kt, :].rearrange("p o q -> p (o q)"),
                                         start=kt == 0, stop=kt == KT - 1)
                last.then_inc(sem["gu_done"], 1)

            def ffn_chunk(c, more=True):
                gate_up(c, 0)
                if more:
                    turn_tile(c + 1, 0)
                    turn_tile(c + 1, 1)
                gate_up(c, 1)
                if more:
                    turn_tile(c + 1, 2)
                gate_up(c, 2)
                if more:
                    turn_tile(c + 1, 3)

            for j in range(JT):
                turn_tile(0, j)
            pe.wait_ge(sem["scale_ready"], 1)
            pe.wait_ge(sem["w2_loaded"], 48)
            ffn_chunk(0)
            with pe.Fori(1, NC - 1) as c:
                ffn_chunk(c)
            ffn_chunk(NC - 1, more=False)
            spread_max(44, sem["hmax_ready"], sem["hmxT_done"], sem["hmxs_ready"], sem["hmxb_done"], 6)

            def down_tile(t, par):
                c = t // JT
                pe.wait_ge(sem["hq_ready"], c + 1)
                if isinstance(t, int) and t < 2:
                    pe.wait_ge(sem["h_ready"], 3 * NC)
                else:
                    pe.wait_ge(sem["y_ready"], t - 1)
                for half in range(2):
                    for i in range(3):
                        last = pe.matmul(ps[0:TP, 2 * par + half, :], hqT[:, i, bass.ds(t * TP, TP)],
                                         wdnT[:, 4 * half:4 * half + 4, i, :], start=i == 0, stop=i == 2)
                last.then_inc(sem["down_done"], 1)

            over_pairs(pe, down_tile)

        @block.scalar
        def _(act):
            own = Own(act, sem["act_own"])

            def weight_hi(raw, hi, slabs, level):
                for kt in range(KT):
                    act.wait_ge(slabs[kt], level)
                    act.activation(hi[:, kt, :], raw[:, kt, :], ACT.Copy).then_inc(sem["w_hi_ready"], 1)

            def root(t, par, n0=0):
                act.wait_ge(sem["var_ready"], n0 + t + 1)
                own.mark(act.activation(rst[:, par, 2:3], rst[:, par, 0:1], ACT.Ln))
                own.settle()
                act.activation(rst[:, par, 1:2], rst[:, par, 2:3], ACT.Exp, scale=-0.5).then_inc(sem["r0_ready"], 1)

            def turned(b=6):
                return ps[:, b:b + 2, 0:JT * TP]

            def x_hi(t, par):
                act.wait_ge(sem["xnT_done"], t + 1)
                after(act, sem["v_done"], t - 1)
                if not (isinstance(t, int) and t < 2):
                    act.wait_ge(xt_stored[par], 2 * half_of(t - 2))
                act.activation(xh[:, par, :].rearrange("p (b c) -> p b c", b=2), turned(), ACT.Copy).then_inc(sem["hi_ready"], 1)

            act.wait_ge(sem["zero_ready"], 1)
            per = CELLS_ALL // P
            cv = cells.ap().rearrange("(p q r f) o -> q p r (f o)", p=P, q=12, f=P)

            cleared = []

            def clear(count):
                for q in range(len(cleared), len(cleared) + count):
                    cleared.append(q)
                    act.dma_start(cv[q], zero[:].unsqueeze(1).to_broadcast([P, per // 12 // P, P])).then_inc(sem["cells_zeroed"], 16)

            act.preload_act_table_set("natural_log_exp_and_others")
            root(0, 0)
            root(1, 1)
            weight_hi(A_raw, A_hi, slab_a, 16)
            x_hi(0, 0)
            clear(1)
            weight_hi(B_raw, B_hi, slab_b, 16)
            clear(1)

            def kv_tile(t, par):
                act.wait_ge(sem["k_done"], t + 1)
                after(act, sem["kv_done"], t - 1)
                act.activation(ebuf[:, par, :], banks(0, 2, TP), ACT.Exp).then_inc(sem["exp_ready"], 1)
                if isinstance(t, int) and t < 2:
                    clear((2, 3)[t])
                if within(t, NT - 1):
                    x_hi(t + 1, 1 - par)
                late = isinstance(t, int) and t < 2
                if within(t, NT - 2) and not late:
                    root(t + 2, par)
                if not within(t, NT - 1):
                    weight_hi(A_raw, A_hi, slab_a, 32)
                act.wait_ge(sem["v_done"], t + 1)
                act.activation(vbuf[:, par, :], banks(2, 2, TP), ACT.Copy).then_inc(sem["v_ready"], 1)
                if late:
                    clear((2, 3)[t])
                    root(t + 2, par)

            over_pairs(act, kv_tile, own)

            act.wait_ge(sem["kv_done"], NT)
            act.wait_ge(sem["ksumb_done"], 1)
            act.activation(ksum_b[:], banks(2, 2, TP), ACT.Copy).then_inc(sem["ksumb_ready"], 1)
            act.wait_ge(sem["kvT_zero"], 1)
            for q in range(2):
                rows_q = slice(q * AD, (q + 1) * AD)
                act.activation(kvT[rows_q, :, rows_q], banks(4, 2).rearrange("p (k d) -> p k d", k=KT)[rows_q, :, rows_q],
                               ACT.Copy).then_inc(sem["kvT_ready"], 1)

            def q_exp(t):
                act.wait_ge(sem["q_done"], t + 1)
                after(act, sem["qT_done"], t)
                act.activation(qbuf[:], banks(0, 2, TP), ACT.Exp).then_inc(sem["exp_ready"], 1)

            def q_high(t):
                act.wait_ge(sem["qT_done"], t + 1)
                after(act, sem["mix_done"], t)
                act.activation(q_hi[:].rearrange("p (b c) -> p b c", b=2), turned(), ACT.Copy).then_inc(sem["qhi_ready"], 1)

            q_exp(0)
            for p in range(KT):
                act.wait_ge(sem["g_done"], p + 1)
                act.activation(B_hi[:, p, :], banks(6 if p % 2 == 0 else 4, 2), ACT.Copy).then_inc(sem["ghi_ready"], 1)
            q_high(0)

            def mix_tile(t, par):
                if within(t, NT - 1):
                    q_exp(t + 1)
                    q_high(t + 1)

            over_pairs(act, mix_tile)
            weight_hi(A_raw, A_hi, slab_a, 48)

            def z_tile(t, par, b):
                if isinstance(t, int) and t == 0:
                    act.wait_ge(sem["mix_done"], NT)
                    act.wait_ge(sem["counted"], NB)
                act.wait_ge(sem["z_done"], t + 1)
                act.activation(z[:, bass.ds(t, 1), :, 0:GF].rearrange("p o h f -> p (o h) f"),
                               banks(2 * par, 2, TP).rearrange("p (h f) -> p h f", h=GH), ACT.Copy).then_inc(sem["z_ready"], 1)
                if b is None:
                    return
                act.wait_ge(wT_stored[par], 16 * (b + 1))
                act.wait_ge(wT_done[par], b + 2)
                bank = ps[:, 6 + par, :].bitcast(BF16)
                if par == 0:
                    act.activation(wturn[:, 0, :], bank, ACT.Copy).then_inc(wT_ready[0], 1)
                else:
                    act.activation(wturn[:, 1, 0:2 * P], bank[:, 0:2 * P], ACT.Copy)
                    act.activation(wturn[0:FI - 2 * P, 1, 2 * P:FIP], bank[0:FI - 2 * P, 2 * P:FIP], ACT.Copy).then_inc(wT_ready[1], 1)

            act.wait_ge(sem["wpad_zero"], 1)
            for par in range(2):
                act.sem_inc(wT_ready[par], 1)
            over_weight_tiles(act, z_tile)

            def spread_out(c, r):
                act.wait_ge(sem["bc_done"], 8 * c + r + 1)
                act.activation(rb[:, bass.ds(c % 2, 1), r, :].rearrange("p o q -> p (o q)"), ps[0:TP, r % 4, 0:CW], ACT.Copy)\
                    .then_inc(sem["rb_ready"], 1)

            def mark_missing(m, counts):
                after(act, sem["nmax_ready"], m - 1)
                if not known_zero(m - 1):
                    apart(act, sem)
                act.activation(no_edge[:, bass.ds(m % 2, 1), :].rearrange("p o q -> p (o q)"), counts, ACT.Exp,
                               scale=-1000.0, bias=far[0:TP, :]).then_inc(sem["ind_ready"], 1)

            def missing_first(i):
                for s in range(4):
                    act.wait_ge(cc_loaded[s], 16 * (i + 1))
                    mark_missing(4 * i + s, cnt_c[:, bass.ds(4 * i + s, 1), :].rearrange("p o q -> p (o q)"))

            def missing(m):
                act.wait_ge(sem["cm_loaded"], 16 * (m - NT + 1))
                mark_missing(m, cnt_m[:, bass.ds(m % 2, 1), :].rearrange("p o q -> p (o q)"))

            act.wait_ge(sem["far_set"], 1)
            missing_first(0)
            with act.Fori(1, NT // 4) as i:
                missing_first(i)
            act.wait_ge(sem["el02_ready"], 1)
            weights_stored(act)
            missing(NT)
            missing(NT + 1)
            for r in range(8):
                spread_out(0, r)
                if r < 3:
                    missing(NT + 2 + r)

            def gat_steps(c, h, u, live, late=False):
                for s in range(4):
                    if s == 1 and live and not late:
                        missing((4 * c + h) * 5 + u + 25)
                    n = ((4 * c + h) * 5 + u) * 2 + s // 2
                    if s % 2 == 0 and not known_zero(n - 1):
                        act.wait_ge(sem["p_ready"], n - 1)
                        apart(act, sem)
                    t = 4 * u + s
                    act.activation(e1[:, s, :], rb[:, bass.ds(c % 2, 1), h, :].rearrange("p o q -> p (o q)"), ACT.Exp,
                                   bias=elr[:, bass.ds(t, 1), h])
                    act.activation(e2[:, s, :], rb[:, bass.ds(c % 2, 1), 4 + h, :].rearrange("p o q -> p (o q)"), ACT.Exp,
                                   bias=el02[:, bass.ds(t, 1), h]).then_inc(sem["e_ready"], 1)

            def gat_chunk(c, left):
                act.wait_ge(sem["rb_ready"], 8 * (c + 1))
                for h in range(GH):
                    live = left >= (1 if h < 3 else 2)
                    if h == 3 and left:
                        for u in range(5):
                            gat_steps(c, h, u, live, late=True)
                            if live:
                                missing((4 * c + h) * 5 + u + 25)
                            if u == 3:
                                for r in range(4):
                                    spread_out(c + 1, r)
                        for r in range(4, 8):
                            spread_out(c + 1, r)
                    elif isinstance(c, int) and c == 0 and h == 0:
                        gat_steps(c, h, 0, live)
                        with act.Fori(1, 5) as u:
                            gat_steps(c, h, u, live)
                    else:
                        with act.Fori(0, 5) as u:
                            gat_steps(c, h, u, live)

            over_chunks(act, gat_chunk)

            act.wait_ge(sem["var_ready"], NT + 1)
            act.activation(rs2[:, 2, :], rs2[:, 0, :], ACT.Ln).then_inc(sem["stats_ready"], 1)
            act.wait_ge(sem["stats_ready"], 1)
            act.activation(rs2[:, 1, :], rs2[:, 2, :], ACT.Exp, scale=-0.5).then_inc(sem["r0_ready"], 1)

            def norm_tiles(i):
                for s in range(4):
                    t = 4 * i + s
                    xt = xn2[:, bass.ds(t, 1), :].rearrange("p o d -> p (o d)")
                    act.wait_ge(x1t_loaded[s], 16 * (i + 1))
                    apart(act, sem)
                    act.activation(xt, xt, ACT.Identity, scale=rs2[:, 3, bass.ds(t, 1)], bias=rs2[:, 2, bass.ds(t, 1)])\
                       .then_inc(sem["xn2_ready"], 1)

            act.wait_ge(sem["rstd_ready"], 1)
            norm_tiles(0)
            with act.Fori(1, NC) as i:
                norm_tiles(i)
            act.wait_ge(sem["clip_loaded"], 32)
            act.activation(tiny[:, 46:48], tiny[:, 40:42], ACT.Exp, scale=-1.0).then_inc(sem["sig_ready"], 1)

            def round_tile(c, j):
                t = 4 * c + j
                if not (isinstance(t, int) and t < 2):
                    act.wait_ge(sem["xint_ready"], t - 1)
                act.activation(xrnd[:, j % 2, :], xn2[:, bass.ds(t, 1), :].rearrange("p o d -> p (o d)"), ACT.Copy,
                               scale=tiny[0:TP, 49:50], bias=MAGIC).then_inc(sem["rnd_ready"], 1)

            def turned_tile(c, j):
                t = 4 * c + j
                act.wait_ge(sem["xqT_done"], t + 1)
                if not (isinstance(c, int) and c < 2):
                    act.wait_ge(sem["gu_done"], 3 * (c - 1))
                act.activation(xqT[:, bass.ds(c % 2, 1), :, j * TP:(j + 1) * TP].rearrange("p o k q -> p (o k) q"),
                               ps[:, 6 + j % 2, :].bitcast(BF16).rearrange("p (k c) -> p k c", c=P)[:, :, 0:TP], ACT.Copy)\
                    .then_inc(sem["xqT_ready"], 1)

            def silu(c, i):
                rows_n = IB[i][1]
                act.wait_ge(sem["gu_done"], 3 * c + i + 1)
                if not known_zero(c):
                    act.wait_ge(sem["h_ready"], 3 * (c - 1) + i + 1)
                act.activation(gsil[0:rows_n, i, :], ps[0:rows_n, 2 * i, 0:CW], ACT.Silu,
                               scale=tiny[0:rows_n, 50 + i:51 + i]).then_inc(sem["sil_ready"], 1)

            def ffn_chunk(c, more=True):
                if more:
                    round_tile(c + 1, 0)
                    round_tile(c + 1, 1)
                    turned_tile(c + 1, 0)
                silu(c, 0)
                if more:
                    round_tile(c + 1, 2)
                    turned_tile(c + 1, 1)
                silu(c, 1)
                if more:
                    round_tile(c + 1, 3)
                    turned_tile(c + 1, 2)
                silu(c, 2)
                if more:
                    turned_tile(c + 1, 3)

            act.wait_ge(sem["scale_ready"], 1)
            round_tile(0, 0)
            round_tile(0, 1)
            turned_tile(0, 0)
            round_tile(0, 2)
            turned_tile(0, 1)
            round_tile(0, 3)
            turned_tile(0, 2)
            turned_tile(0, 3)
            ffn_chunk(0)
            with act.Fori(1, NC - 1) as c:
                ffn_chunk(c)
            ffn_chunk(NC - 1, more=False)

            act.wait_ge(sem["hscale_ready"], 1)
            with act.Fori(0, NC) as c:
                hc = hT[:, :, bass.ds(c * CW, CW)]
                act.activation(hc, hc, ACT.Copy, scale=tiny[:, 57:58], bias=MAGIC).then_inc(sem["hrnd_ready"], 1)

        @block.vector
        def _(dve):
            own = Own(dve, sem["dve_own"])

            def weight_lo(raw, hi, lo, base):
                for kt in range(KT):
                    dve.wait_ge(sem["w_hi_ready"], base + kt + 1)
                    dve.tensor_tensor(lo[:, kt, :], raw[:, kt, :], hi[:, kt, :].bitcast(F32), ALU.subtract)\
                       .then_inc(sem["w_lo_ready"], 1)

            def statistics(source, par):
                for half in range(2):
                    ins = dve.bn_stats(stats[:, half, :], source[:, half * HALF:(half + 1) * HALF])
                own.mark(ins)
                own.settle()
                apart(dve, sem)
                own.mark(dve.bn_aggr(mv[:, par, :], stats[:]))
                own.settle()
                dve.tensor_scalar(rst[:, par, 0:1], mv[:, par, 1:2], EPS, None, ALU.add).then_inc(sem["var_ready"], 1)

            def refine(t, par, n0=0):
                dve.wait_ge(sem["r0_ready"], n0 + t + 1)
                own.mark(dve.tensor_tensor(rst[:, par, 2:3], rst[:, par, 1:2], rst[:, par, 1:2], ALU.mult))
                own.settle()
                own.mark(dve.tensor_tensor(rst[:, par, 2:3], rst[:, par, 2:3], rst[:, par, 0:1], ALU.mult))
                own.settle()
                own.mark(dve.tensor_scalar(rst[:, par, 2:3], rst[:, par, 2:3], -0.5, 1.5, ALU.mult, ALU.add))
                own.settle()
                own.mark(dve.tensor_tensor(rst[:, par, 3:4], rst[:, par, 1:2], rst[:, par, 2:3], ALU.mult))
                own.settle()

            def normalise(out_ap, source, par):
                return dve.tensor_scalar(out_ap, source, mv[:, par, 0:1], rst[:, par, 3:4], ALU.subtract, ALU.mult)

            def x_stats(t, par):
                dve.wait_ge(x_loaded[par], half_of(t))
                statistics(xbuf[:, par, :], par)

            def x_norm(t, par):
                refine(t, par)
                after(dve, sem["xnT_done"], t)
                normalise(xn[:], xbuf[:, par, :], par).then_inc(sem["xn_ready"], 1)

            def x_lo(t, par):
                dve.wait_ge(sem["hi_ready"], t + 1)
                dve.tensor_tensor(xl[:, par, :].rearrange("p (b c) -> p b c", b=2), ps[:, 6:8, 0:JT * TP],
                                  xh[:, par, :].bitcast(F32).rearrange("p (b c) -> p b c", b=2), ALU.subtract)\
                   .then_inc(sem["lo_ready"], 1)

            x_stats(0, 0)
            dve.wait_ge(sem["edges_loaded"], 32)
            dve.scalar_tensor_tensor(out=key_f[:], in0=src_i[:], scalar=float(N), in1=dst_i[:], op0=ALU.mult, op1=ALU.add)\
               .then_inc(sem["key_ready"], 1)
            dve.wait_ge(sem["consts_ready"], 2)
            dve.tensor_copy(pad_f[:], pad_i[:]).then_inc(sem["key_ready"], 1)
            dve.tensor_copy(own_cell[:], dummy_i[:]).then_inc(sem["key_ready"], 1)
            x_norm(0, 0)
            x_stats(1, 1)
            dve.wait_ge(sem["keysT_done"], 1)
            for a in range(5):
                dve.tensor_copy(keycol[:, 0:EROWS].rearrange("q (p a) -> q a p", a=5)[:, a, :],
                                ps[:, 4 + a // 4, (a % 4) * TP:(a % 4 + 1) * TP])
            dve.tensor_copy(keycol[:, EROWS:NB * COLS], ps[:, 5, TP:TP + 15]).then_inc(sem["keycol_ready"], 1)
            dve.memset(ksum[:], 0.0).then_inc(sem["ksum_done"], 1)
            weight_lo(A_raw, A_hi, A_lo, 0)
            x_lo(0, 0)
            weight_lo(B_raw, B_hi, B_lo, KT)
            dve.wait_ge(sem["keycol_ready"], 1)
            dve.wait_ge(sem["key_ready"], 3)
            dve.wait_ge(sem["consts_ready"], 4)

            kc = tiny[:, 0:COLS]
            cn = tiny[:, COLS:2 * COLS]

            def dedupe(b, par, groups):
                if groups[0][0] == 0:
                    own.mark(dve.tensor_copy(kc, keycol[:, bass.ds(b * COLS, COLS)]))
                    own.settle()
                    dve.wait_ge(keyrow_loaded[par], half_of(b))
                for first, end in groups:
                    for q in range(first, end):
                        place = (WIDEST - 1 - (q - first)) * P
                        own.settle(1)
                        ins = dve.scalar_tensor_tensor(out=junk[:, q % 2, 0:(end - first) * P], in0=keyrow[:, par, first * P:end * P],
                                                       scalar=tiny[:, q:q + 1], in1=first_w[:, place:place + (end - first) * P], op0=ALU.is_equal,
                                                        op1=ALU.mult, accum_out=tiny[:, COLS + q:COLS + q + 1])
                        if q == COLS - 1:
                            ins.then_inc(sem["counted"], 1)
                        else:
                            own.mark(ins)
                if groups[-1][1] < COLS:
                    return
                dve.wait_ge(sem["counted"], b + 1)
                dve.tensor_scalar(is_first[:], cn, 1000.0, None, ALU.is_lt)
                dve.tensor_tensor(key_off[:], kc, own_cell[:], ALU.subtract)
                own.mark(dve.tensor_copy(count[:, bass.ds(b * COLS, COLS)], cn))
                own.settle()
                own.mark(dve.tensor_tensor(key_off[:], key_off[:], is_first[:], ALU.mult))
                own.settle()
                dve.tensor_tensor(cell[:, bass.ds(b * COLS, COLS)], key_off[:], own_cell[:], ALU.add).then_inc(sem["cell_ready"], 1)

            def phi(buf, t, n0, ready):
                dve.wait_ge(sem["exp_ready"], n0 + t + 1)
                dve.tensor_scalar(buf, buf, 1.0, None, ALU.min).then_inc(sem["kmin_ready"], 1)
                dve.wait_ge(sem["kmin_ready"], n0 + t + 1)
                dve.scalar_tensor_tensor(out=buf, in0=banks(0, 2, TP), scalar=1.0, in1=buf, op0=ALU.add, op1=ALU.max)\
                   .then_inc(ready, 1)
                dve.wait_ge(ready, t + 1)

            def kv_tile(t, par):
                if within(t, NT - 1):
                    x_norm(t + 1, 1 - par)
                early = isinstance(t, int) and t == 0
                if not early:
                    dedupe(t, par, KV_GROUPS[:2])
                phi(ebuf[:, par, :], t, 0, sem["k_ready"])
                dve.wait_ge(sem["ksum_done"], t + 1)
                dve.tensor_tensor(ksum[:], ksum[:], ebuf[:, par, :], ALU.add).then_inc(sem["ksum_done"], 1)
                if within(t, NT - 1):
                    x_lo(t + 1, 1 - par)
                if within(t, NT - 2):
                    x_stats(t + 2, par)
                if not within(t, NT - 1):
                    weight_lo(A_raw, A_hi, A_lo, 2 * KT)
                dedupe(t, par, KV_GROUPS if early else KV_GROUPS[2:])

            over_pairs(dve, kv_tile, own)

            dve.wait_ge(sem["kv_done"], NT)
            dve.memset(kvT[:], 0.0).then_inc(sem["kvT_zero"], 1)

            def q_phi(t):
                phi(qbuf[:], t, NT, sem["q_ready"])
                if isinstance(t, int) and t == 0:
                    dve.wait_ge(sem["ksumb_ready"], 1)
                own.mark(dve.tensor_tensor(qk[:], qbuf[:], ksum_b[:], ALU.mult))
                own.settle()
                den = tiny[0:TP, 32:48]
                own.mark(dve.tensor_reduce(den, qk[:].rearrange("p (h d) -> p h d", h=AH), AX.X, ALU.add))
                own.settle()
                own.mark(dve.tensor_scalar(den, den, 1e-8, None, ALU.add))
                own.settle()
                own.mark(dve.reciprocal(den, den))
                own.settle()
                dve.tensor_tensor(qbuf[:].rearrange("p (h d) -> p h d", h=AH), qbuf[:].rearrange("p (h d) -> p h d", h=AH),
                                  den.unsqueeze(2).to_broadcast([TP, AH, AD]), ALU.mult).then_inc(sem["qs_ready"], 1)

            def q_low(t):
                dve.wait_ge(sem["qhi_ready"], t + 1)
                dve.tensor_tensor(q_lo[:].rearrange("p (b c) -> p b c", b=2), ps[:, 6:8, 0:JT * TP],
                                  q_hi[:].bitcast(F32).rearrange("p (b c) -> p b c", b=2), ALU.subtract).then_inc(sem["qlo_ready"], 1)

            q_phi(0)
            for p in range(KT):
                dve.wait_ge(sem["ghi_ready"], p + 1)
                dve.tensor_tensor(B_lo[:, p, :], banks(6 if p % 2 == 0 else 4, 2), B_hi[:, p, :].bitcast(F32), ALU.subtract)\
                   .then_inc(sem["glo_ready"], 1)
            q_low(0)
            dve.wait_ge(sem["bias_loaded"], 16)

            def mix_tile(t, par):
                dedupe(NT + t, par, MIX_GROUPS[:2])
                dve.wait_ge(x2_loaded[par], half_of(t))
                dve.tensor_tensor(xbuf[:, par, :], xbuf[:, par, :], bias_b[:], ALU.add).then_inc(sem["xb_ready"], 1)
                if within(t, NT - 1):
                    q_phi(t + 1)
                dedupe(NT + t, par, MIX_GROUPS[2:3])
                if not within(t, NT - 1):
                    weight_lo(A_raw, A_hi, A_lo, 3 * KT)
                dve.wait_ge(sem["mix_done"], t + 1)
                dve.wait_ge(sem["xb_ready"], t + 1)
                dve.tensor_tensor(xbuf[:, par, :], banks(2, 2, TP), xbuf[:, par, :], ALU.add).then_inc(sem["x1_ready"], 1)
                if within(t, NT - 1):
                    q_low(t + 1)
                dedupe(NT + t, par, MIX_GROUPS[3:])

            over_pairs(dve, mix_tile, own)

            dve.wait_ge(sem["mix_done"], NT)
            dve.memset(z[:, :, :, GF:ZW].rearrange("p t h f -> p (t h) f"), 1.0).then_inc(sem["z_ones"], 1)
            dve.wait_ge(sem["xb_ready"], NT)
            dve.memset(wturn[:, 1, 2 * P:FIP], 0.0).then_inc(sem["wpad_zero"], 1)
            dve.wait_ge(sem["a_loaded"], 16)

            def quantise(par, b):
                cols = (D, FI)[par]
                row = wrow[:, par, 0:cols]
                sc, rs = wsc[:, 0:1], wsc[:, 1:2]
                dve.wait_ge(wrow_loaded[par], 16 * (b + 1))
                own.mark(dve.tensor_reduce(sc, row, AX.X, ALU.max, apply_absolute_value=True))
                own.settle()
                own.mark(dve.tensor_scalar(sc, sc, 1.0 / QMAX, None, ALU.mult))
                own.settle()
                own.mark(dve.reciprocal(rs, sc))
                own.mark(dve.tensor_copy(wscale[:, bass.ds(b if par == 0 else GU + b, 1)], sc))
                own.settle()
                own.mark(dve.tensor_scalar(row, row, rs, MAGIC, ALU.mult, ALU.add))
                own.settle()
                dve.wait_ge(wT_done[par], b + 1)
                own.mark(dve.tensor_scalar(wint[:, par, 0:cols], row, -MAGIC, QMAX, ALU.add, ALU.min))
                own.settle()
                dve.tensor_scalar(wint[:, par, 0:cols], wint[:, par, 0:cols], -QMAX - 1.0, None, ALU.max).then_inc(wint_ready[par], 1)

            def z_tile(t, par, b):
                if b is not None:
                    quantise(par, b)
                dve.wait_ge(sem["z_ready"], t + 1)
                after(dve, sem["el_ready"], t)
                for r in range(2):
                    for h in range(GH):
                        q = 4 * r + h
                        own.settle(1)
                        own.mark(dve.scalar_tensor_tensor(out=junk[0:TP, q % 2, 0:GF], in0=z[:, bass.ds(t, 1), h, 0:GF].rearrange("p o f -> p (o f)"),
                                                          scalar=1.0, in1=a_b[:, r, h * GF:(h + 1) * GF], op0=ALU.mult, op1=ALU.mult,
                                                          accum_out=tiny[0:TP, 48 + q:49 + q]))
                own.settle()
                dve.tensor_copy(elr[:, bass.ds(t, 1), :].rearrange("p o q -> p (o q)"), tiny[0:TP, 48:56]).then_inc(sem["el_ready"], 1)

            own.pair = {True: 2 * 8 + 2 * 6, False: 2 * 8 + 6}
            over_weight_tiles(dve, z_tile, own)
            own.settle()
            dve.wait_ge(sem["el_ready"], NT)
            dve.sem_inc(sem["scales_ready"], 1)
            dve.tensor_scalar(el02[:], elr[:, :, 0:GH], SLOPE, None, ALU.mult).then_inc(sem["el02_ready"], 1)

            def start_maxima(c):
                after(dve, sem["nmaxT_done"], c)

            def maxima_head(m, h, first=False):
                if h == 0:
                    dve.wait_ge(sem["ind_ready"], m + 1)
                    after(dve, sem["nmax_ready"], m)
                if first:
                    ins = dve.tensor_scalar(nmin[:, h, :], no_edge[:, bass.ds(m % 2, 1), :].rearrange("p o c -> p (o c)"),
                                            elr[:, bass.ds(m % NT, 1), h], None, ALU.subtract)
                else:
                    ins = dve.scalar_tensor_tensor(out=nmin[:, h, :], in0=no_edge[:, bass.ds(m % 2, 1), :].rearrange("p o c -> p (o c)"),
                                               scalar=elr[:, bass.ds(m % NT, 1), h], in1=nmin[:, h, :],
                                               op0=ALU.subtract, op1=ALU.min)
                if h == GH - 1:
                    ins.then_inc(sem["nmax_ready"], 1)

            def maxima_tile(m, first=False):
                for h in range(GH):
                    maxima_head(m, h, first)

            def finish_maxima(c):
                mx = tiny[0:TP, 0:16].rearrange("p (j h) -> p j h", j=JT)
                mx2 = tiny[0:TP, 16:32].rearrange("p (j h) -> p j h", j=JT)
                er = elr[:, bass.ds(4 * c, 4), 4:8]
                dve.wait_ge(sem["nmaxT_done"], c + 1)
                own.mark(dve.tensor_reduce(mx, ps[0:TP, 0:JT, 0:GH * TP].rearrange("p j (h q) -> p j h q", h=GH), AX.X, ALU.min))
                own.settle()
                own.mark(dve.tensor_tensor(mx, er, mx, ALU.subtract))
                own.settle()
                own.mark(dve.scalar_tensor_tensor(out=mx2, in0=mx, scalar=SLOPE, in1=mx, op0=ALU.mult, op1=ALU.max))
                own.settle()
                after(dve, sem["bc_done"], 8 * c)
                dve.tensor_tensor(rr[:, 0:4, :].rearrange("p h j -> p j h"), er, mx2, ALU.subtract)
                dve.scalar_tensor_tensor(out=rr[:, 4:8, :].rearrange("p h j -> p j h"), in0=er, scalar=SLOPE, in1=mx2,
                                         op0=ALU.mult, op1=ALU.subtract).then_inc(sem["rr_ready"], 1)

            weights_stored(dve)
            start_maxima(0)
            def maxima_tiles(i):
                for s in range(4):
                    maxima_tile(4 * i + s, known_zero(4 * i + s))

            own.loop(0, NT // 4, maxima_tiles)
            finish_maxima(0)
            start_maxima(1)
            for m in range(NT, NT + 5):
                maxima_tile(m, m == NT)

            def larger(n, k):
                dve.wait_ge(sem["e_ready"], 2 * n + 2)
                two = slice(2 * k, 2 * k + 2)
                dve.tensor_tensor(e1[:, two, :], e1[:, two, :], e2[:, two, :], ALU.max).then_inc(sem["emax_ready"], 1)

            def weigh(n, k, c, u):
                two = slice(2 * k, 2 * k + 2)
                dve.wait_ge(sem["emax_ready"], n + 1)
                after(dve, sem["p_used"], 2 * n - 2)
                for s in range(2 * k, 2 * k + 2):
                    dve.wait_ge(cc_loaded[s], 16 * (5 * c + u + 1))
                dve.scalar_tensor_tensor(out=prob[:, two, :], in0=e1[:, two, :], scalar=1.0,
                                         in1=cnt_c[:, bass.ds(4 * u + 2 * k, 2), :], op0=ALU.min, op1=ALU.mult)\
                   .then_inc(sem["p_ready"], 1)

            def head_out(c, h):
                n = 4 * c + h
                dve.wait_ge(sem["p_used"], NT * (n + 1))
                total = tiny[0:TP, 32:36]
                own.mark(dve.tensor_scalar(total, ps[0:TP, 4 * (h % 2):4 * (h % 2) + 4, GF:ZW].rearrange("p j o -> p (j o)"),
                                           1e-30, None, ALU.max))
                own.settle()
                own.mark(dve.reciprocal(total, total))
                own.settle()
                dve.wait_ge(x1c_loaded[h % 2], 16 * (2 * c + h // 2 + 1))
                for j in range(JT):
                    last = dve.scalar_tensor_tensor(out=x1c[:, h % 2, j, :], in0=ps[0:TP, 4 * (h % 2) + j, 0:GF],
                                                    scalar=tiny[0:TP, 32 + j:33 + j], in1=x1c[:, h % 2, j, :],
                                                    op0=ALU.mult, op1=ALU.add)
                own.mark(last)
                own.settle()
                for j in range(JT):
                    last = dve.bn_stats(st2[:, j, h, :], x1c[:, h % 2, j, :])
                last.then_inc(sem["x1c_ready"], 1)
                if h == GH - 1:
                    dve.wait_ge(sem["x1c_ready"], n + 1)
                    apart(dve, sem)
                    for j in range(JT):
                        last = dve.bn_aggr(mvc[:, j, :], st2[:, j, :, :].rearrange("p h s -> p (h s)"))
                    own.mark(last)
                    own.settle()
                    own.mark(dve.tensor_copy(mv2[:, bass.ds(JT * c, JT), :], mvc[:]))

            def gat_steps(c, h, u, tiles, first=False):
                n = ((4 * c + h) * 5 + u) * 2
                heads = [(m, q, first and i == 0) for i, m in enumerate(tiles) for q in range(GH)]

                def some(count):
                    for m, q, f in heads[:count]:
                        maxima_head(m, q, f)
                    del heads[:count]

                larger(n, 0)
                some(len(tiles))
                weigh(n, 0, c, u)
                some(len(tiles))
                larger(n + 1, 1)
                some(2 * len(tiles))
                weigh(n + 1, 1, c, u)

            def gat_chunk(c, left):
                for h in range(GH):
                    live = left >= (1 if h < 3 else 2)
                    m = (4 * c + h) * 5 + 25
                    turns = h == 3 and left
                    gat_steps(c, h, 0, [m] if live and not turns else [])
                    if not (known_zero(c) and h == 0):
                        head_out(c - 1 if h == 0 else c, (h - 1) % GH)
                    if not turns:
                        own.loop(1, 5, lambda u: gat_steps(c, h, u, [m + u] if live else []))
                        continue
                    gat_steps(c, h, 1, [])
                    finish_maxima(c + 1)
                    if live:
                        start_maxima(c + 2)
                    gat_steps(c, h, 2, [m, m + 1] if live else [], first=True)
                    gat_steps(c, h, 3, [m + 2] if live else [])
                    gat_steps(c, h, 4, [m + 3, m + 4] if live else [])

            over_chunks(dve, gat_chunk, own, more=5)
            head_out(NC - 1, GH - 1)

            dve.wait_ge(sem["x1c_ready"], GH * NC)
            own.mark(dve.memset(tiny[:], 0.0))
            own.settle()
            own.mark(dve.memset(amax[:], 0.0))
            dve.sem_inc(sem["clip_free"], 1)
            dve.tensor_scalar(rs2[:, 0, :], mv2[:, :, 1], EPS, None, ALU.add).then_inc(sem["var_ready"], 1)
            dve.wait_ge(sem["r0_ready"], NT + 1)
            own.mark(dve.tensor_tensor(rs2[:, 2, :], rs2[:, 1, :], rs2[:, 1, :], ALU.mult))
            own.settle()
            own.mark(dve.tensor_tensor(rs2[:, 2, :], rs2[:, 2, :], rs2[:, 0, :], ALU.mult))
            own.settle()
            own.mark(dve.tensor_scalar(rs2[:, 2, :], rs2[:, 2, :], -0.5, 1.5, ALU.mult, ALU.add))
            own.settle()
            own.mark(dve.tensor_tensor(rs2[:, 3, :], rs2[:, 1, :], rs2[:, 2, :], ALU.mult))
            own.settle()

            dve.scalar_tensor_tensor(out=rs2[:, 2, :], in0=mv2[:, :, 0], scalar=-1.0, in1=rs2[:, 3, :], op0=ALU.mult, op1=ALU.mult)\
               .then_inc(sem["rstd_ready"], 1)

            def norm_tiles(i):
                for s in range(4):
                    t = 4 * i + s
                    dve.wait_ge(sem["xn2_ready"], t + 1)
                    ins = dve.tensor_reduce(amax[0:TP, bass.ds(t, 1)], xn2[:, bass.ds(t, 1), :].rearrange("p o d -> p (o d)"),
                                            AX.X, ALU.max, apply_absolute_value=True)
                own.mark(ins)

            own.loop(0, NC, norm_tiles)
            dve.wait_ge(sem["sig_ready"], 1)
            own.mark(dve.tensor_scalar(tiny[:, 46:48], tiny[:, 46:48], 1.0, None, ALU.add))
            own.settle()
            own.mark(dve.reciprocal(tiny[:, 46:48], tiny[:, 46:48]))
            own.settle()
            own.mark(dve.tensor_scalar(tiny[:, 46:48], tiny[:, 46:48], 1.0 / QMAX, None, ALU.mult))
            own.settle()

            def scale_of(cols, col, max_ready, turned, m_ready, done, bank, sig, out_ready):
                dve.tensor_reduce(tiny[:, col:col + 1], amax[:, 0:cols], AX.X, ALU.max).then_inc(max_ready, 1)
                dve.wait_ge(turned, 1)
                dve.tensor_reduce(tiny[0:1, col + 1:col + 2], ps[0:1, bank, 0:P], AX.X, ALU.max).then_inc(m_ready, 1)
                dve.wait_ge(done, 1)
                own.mark(dve.tensor_tensor(tiny[:, out_ready:out_ready + 1], ps[:, bank, P:P + 1], tiny[:, sig:sig + 1], ALU.mult))
                own.settle()
                ins = dve.reciprocal(tiny[:, out_ready + 1:out_ready + 2], tiny[:, out_ready:out_ready + 1])
                return ins

            own.mark(scale_of(NT, 42, sem["xmax_ready"], sem["mxT_done"], sem["mxs_ready"], sem["mxb_done"], 0, 46, 48))
            own.mark(dve.tensor_scalar(tiny[:, 50:56], wscale[:, 0:6], tiny[:, 48:49], None, ALU.mult))
            own.settle()
            dve.memset(amax[:], 0.0).then_inc(sem["scale_ready"], 1)
            dve.wait_ge(sem["pads_zero"], 1)
            dve.wait_ge(sem["scale_ready"], 1)

            def clip_tile(c, j):
                t = 4 * c + j
                dve.wait_ge(sem["rnd_ready"], t + 1)
                after(dve, sem["xqT_done"], t - 1)
                own.mark(dve.tensor_scalar(xint[:, j % 2, :], xrnd[:, j % 2, :], -MAGIC, QMAX, ALU.add, ALU.min))
                own.settle()
                dve.tensor_scalar(xint[:, j % 2, :], xint[:, j % 2, :], -QMAX - 1.0, None, ALU.max).then_inc(sem["xint_ready"], 1)

            def hidden(c, i):
                rows_n = IB[i][1]
                dve.wait_ge(sem["sil_ready"], 3 * c + i + 1)
                hc = hT[0:rows_n, i, bass.ds(c * CW, CW)]
                dve.scalar_tensor_tensor(out=hc, in0=ps[0:rows_n, 2 * i + 1, 0:CW], scalar=tiny[0:rows_n, 53 + i:54 + i],
                                         in1=gsil[0:rows_n, i, :], op0=ALU.mult, op1=ALU.mult).then_inc(sem["h_ready"], 1)
                dve.wait_ge(sem["h_ready"], 3 * c + i + 1)
                own.mark(dve.tensor_reduce(amax[0:rows_n, bass.ds(3 * c + i, 1)], hc, AX.X, ALU.max, apply_absolute_value=True))

            def ffn_chunk(c, more=True):
                if more:
                    clip_tile(c + 1, 0)
                    clip_tile(c + 1, 1)
                hidden(c, 0)
                if more:
                    clip_tile(c + 1, 2)
                hidden(c, 1)
                if more:
                    clip_tile(c + 1, 3)
                hidden(c, 2)

            for j in range(JT):
                clip_tile(0, j)
            own.loop(0, NC - 1, ffn_chunk)
            ffn_chunk(NC - 1, more=False)
            own.settle()
            scale_of(3 * NC, 44, sem["hmax_ready"], sem["hmxT_done"], sem["hmxs_ready"], sem["hmxb_done"], 6, 47, 56)\
                .then_inc(sem["hscale_ready"], 1)

            def hidden_round(c):
                hc = hT[:, :, bass.ds(c * CW, CW)]
                dve.wait_ge(sem["hrnd_ready"], c + 1)
                hq = hqT[:, :, bass.ds(c * CW, CW)]
                own.mark(dve.tensor_scalar(hq, hc, -MAGIC, QMAX, ALU.add, ALU.min))
                own.settle()
                dve.tensor_scalar(hq, hq, -QMAX - 1.0, None, ALU.max).then_inc(sem["hq_ready"], 1)

            own.loop(0, NC, hidden_round)

            def down_tile(t, par):
                dve.wait_ge(sem["down_done"], t + 1)
                if not (isinstance(t, int) and t < 2):
                    dve.wait_ge(out_ready[par], t // 2)
                dve.scalar_tensor_tensor(out=y[:, par, :], in0=banks(2 * par, 2, TP), scalar=tiny[0:TP, 56:57], in1=sdb[:],
                                         op0=ALU.mult, op1=ALU.mult).then_inc(sem["y_ready"], 1)
                if par:
                    dve.wait_ge(sem["y_ready"], t + 1)
                    dve.wait_ge(xr_loaded[par], half_of(t))
                    xt = xn2[:, bass.ds(t, 1), :].rearrange("p o d -> p (o d)")
                    dve.tensor_tensor(xt, xt, y[:, par, :], ALU.add).then_inc(out_ready[par], 1)

            over_pairs(dve, down_tile)


def kernel(**inputs):
    import numpy as _np
    import concourse.bacc as _bacc
    from concourse import mybir as _mybir
    from concourse.bass_utils import run_bass_kernel_spmd as _run

    given = {k: _np.asarray(v) for k, v in inputs.items()}
    laid = {
        "x": given["x"], "src": given["src"], "dst": given["dst"],
        "w_gat": given["L0_gnn_W"].transpose(1, 0, 2).reshape(D, GH * GF),
        "a_lr": _np.stack([given["L0_gnn_a_l"].reshape(-1), given["L0_gnn_a_r"].reshape(-1)]),
        "w_qkv_t": given["L0_mix_w_qkv"].T, "w_proj_t": given["L0_mix_w_proj"].T, "b_proj": given["L0_mix_b_proj"],
        "clip_x": given["L0_ffn_clip_x"], "clip_down": given["L0_ffn_clip_down"],
        "w_gu": _np.concatenate([a for w in (given["L0_ffn_w_gate"], given["L0_ffn_w_up"]) for a in (w, w[:FIP - FI])]),
        "w_down": given["L0_ffn_w_down"],
    }
    nc = _bacc.Bacc("TRN2", target_bir_lowering=False, num_devices=1)
    arrays, args = {}, []
    for name, a in laid.items():
        a = _np.ascontiguousarray(a)
        arrays[f"in_{name}"] = a
        args.append(nc.dram_tensor(f"in_{name}", a.shape, _mybir.dt.from_np(a.dtype), kind="ExternalInput").ap())
    args.append(nc.dram_tensor("out_0", (N, D), F32, kind="ExternalOutput").ap())
    build(nc, *args)
    r = _run(nc, [arrays], core_ids=[0])
    return r.results[0]["out_0"]
```
